# Optimizing a Trainium2 kernel written in Bass

```python
import numpy as np
import jax
import jax.numpy as jnp

def _softmax(x, axis=-1):
    return jax.nn.softmax(x, axis=axis)

def _gelu(x):
    return jax.nn.gelu(x, approximate=True)

def _silu(x):
    return jax.nn.silu(x)

def _sigmoid(x):
    return jax.nn.sigmoid(x)

def _layernorm(x, axis=-1, eps=1e-05):
    m = jnp.mean(x, axis=axis, keepdims=True)
    v = jnp.var(x, axis=axis, keepdims=True)
    return (x - m) / jnp.sqrt(v + eps)

def _scatter_add(tgt, idx, src, axis=0):
    return tgt.at[idx].add(src)

def _segment_sum(src, seg, n):
    return jax.ops.segment_sum(src, seg, n)
kernel_name = 'mk_gnn_resnorm_d1_gnn_r32_d72b6d'

def setup_inputs(seed: int=0):
    np.random.seed(seed)
    _w = jnp.asarray

    def _rec_inputs():
        import jax
        import jax.numpy as jnp
        _gk = jax.random.key(seed)
        x = -0.000202 + 1 * jax.random.normal(jax.random.fold_in(_gk, 1), (50000, 128), jnp.float32)
        src = jax.random.randint(jax.random.fold_in(_gk, 2), (25000,), 0, 50000, jnp.int32)
        dst = jax.random.randint(jax.random.fold_in(_gk, 3), (25000,), 0, 50000, jnp.int32)
        _o = jnp.argsort(dst, stable=True)
        src = src[_o]
        dst = dst[_o]
        edge_attr_128 = -5.16925e-05 + 1.00005 * jax.random.normal(jax.random.fold_in(_gk, 11), (25000, 128), jnp.float32)
        return (x, src, dst, edge_attr_128)
    x, src, dst, edge_attr_128 = _rec_inputs()

    def _L0_gnn_setup():
        import jax, jax.numpy as jnp
        import numpy as np
        N, E, D, P = (50000, 25000, 128, 4)

        def phm_linear(h, phm_rule, W, bias):
            H = jnp.einsum('nij,nab->iajb', phm_rule, W).reshape(D, D)
            return h @ H + bias
        key = jax.random.key(seed)
        ks = jax.random.split(key, 5)
        x = jax.random.normal(ks[0], (N, D), jnp.float32)
        edge_index = jax.random.randint(ks[1], (2, E), 0, N, dtype=jnp.int32).astype(jnp.int64)
        edge_attr = jax.random.normal(ks[2], (E, D), jnp.float32)
        phm_rule = jax.random.normal(ks[3], (P, P, P), jnp.float32)
        W = jax.random.normal(ks[4], (P, D // P, D // P), jnp.float32) * np.float32(1.0 / np.sqrt(D))
        bias = jnp.zeros((D,), jnp.float32)
        beta = jnp.ones((), jnp.float32)
        return dict(x=x, edge_attr=edge_attr, phm_rule=phm_rule, W=W, bias=bias, beta=beta, edge_index=edge_index)
    _L0_gnn_all = _L0_gnn_setup()
    _L0_gnn_in = {k: v for k, v in _L0_gnn_all.items() if k in ('phm_rule', 'W', 'bias', 'beta')}
    del _L0_gnn_all
    return {'x': x, 'src': src, 'dst': dst, 'edge_attr_128': edge_attr_128, 'L0_gnn_phm_rule': _L0_gnn_in['phm_rule'], 'L0_gnn_W': _L0_gnn_in['W'], 'L0_gnn_bias': _L0_gnn_in['bias'], 'L0_gnn_beta': _L0_gnn_in['beta']}

def reference(x, src, dst, edge_attr_128, L0_gnn_phm_rule, L0_gnn_W, L0_gnn_bias, L0_gnn_beta):
    import jax
    import jax.numpy as jnp

    def _L0_gnn_ref(x, edge_attr, phm_rule, W, bias, beta, edge_index):
        import jax, jax.numpy as jnp
        import numpy as np
        N, E, D, P = (50000, 25000, 128, 4)

        def phm_linear(h, phm_rule, W, bias):
            H = jnp.einsum('nij,nab->iajb', phm_rule, W).reshape(D, D)
            return h @ H + bias
        src, dst = (edge_index[0], edge_index[1])
        msg = x[src] + edge_attr
        s = msg * beta
        m = jax.ops.segment_max(s, dst, num_segments=N)
        e = jnp.exp(s - m[dst])
        denom = jax.ops.segment_sum(e, dst, num_segments=N)
        alpha = e / denom[dst]
        agg = jax.ops.segment_sum(msg * alpha, dst, num_segments=N)
        out = phm_linear(agg, phm_rule, W, bias)
        return out + x
    edge_index = jnp.stack([src, dst])
    x = _layernorm(x + _L0_gnn_ref(x, edge_attr_128, L0_gnn_phm_rule, L0_gnn_W, L0_gnn_bias, L0_gnn_beta, edge_index), axis=-1)
    return x

_drawn_inputs = setup_inputs


def setup_inputs(seed=0):
    import zlib

    import numpy as np

    out = dict(_drawn_inputs(seed))
    spreads = {'L0_gnn_bias': (0.0, 0.1)}
    factors = {}
    for name, (base, spread) in spreads.items():
        noise = np.random.default_rng([zlib.crc32(name.encode()), seed]).standard_normal(out[name].shape)
        drawn = base * np.exp(spread * noise) if base else spread * noise
        out[name] = jnp.asarray(drawn.astype(out[name].dtype))
    for name, factor in factors.items():
        out[name] = (out[name] * factor).astype(out[name].dtype)
    return out
```

```python
import concourse.bass as bass
from concourse import mybir
from contextlib import ExitStack

P = 128
SLOTS = 3
SUB = 4
CHUNK = SUB * P
HALF = SUB * P
SLAB = 2 * HALF
PROLOGUE = 2
PAD_DST = 65535
HUGE = 3.3e38
EPS = 1e-5


def gnn_kernel(nc, x, src, dst, edge_attr, phm_rule, W, bias, beta, out):
    f32, bf16, i32 = mybir.dt.float32, mybir.dt.bfloat16, mybir.dt.int32
    ALU, ACT, AX = mybir.AluOpType, mybir.ActivationFunctionType, mybir.AxisListType

    N, D = x.shape
    E = src.shape[0]
    CHUNKS = -(-E // CHUNK)
    TAIL_EDGES = E - (CHUNKS - 1) * CHUNK
    TAIL_ROWS = TAIL_EDGES // SUB
    EDGE_TILES = CHUNKS * SUB
    HEAP = EDGE_TILES // 2
    SLABS = N // SLAB
    TAIL_NODES = N - SLABS * SLAB
    NODE_TILES = (SLABS + 1) * SLAB // P
    TILES_IN_SLAB = SLAB // P
    ITERATIONS = CHUNKS + 3
    FIRST_SLABS = 5
    PH = phm_rule.shape[0]
    KR = D // PH
    assert D == P and TAIL_EDGES % SUB == 0 and HALF < TAIL_NODES < SLAB and N < PAD_DST

    ctx = ExitStack()
    with ctx:
        def sb(name, shape, dt=f32):
            return ctx.enter_context(nc.sbuf_tensor(name, shape, dt))

        def pb(name, shape):
            return ctx.enter_context(nc.psum_tensor(name, shape, f32))

        def sem(name):
            return ctx.enter_context(nc.semaphore(name))

        z = sb("z", [P, EDGE_TILES + 1, D])
        last_dst = sb("last_dst", [P, EDGE_TILES + 1])
        edge_rows = sb("edge_rows", [P, 2, CHUNK], bf16)
        slab_schedule = sb("slab_schedule", [1, 56], i32)
        first_tile = sb("first_tile", [1, NODE_TILES], i32)
        end_tile = sb("end_tile", [1, NODE_TILES], i32)
        extra_before = sb("extra_before", [1, NODE_TILES], i32)
        wide_flag = sb("wide_flag", [1, 1], i32)
        H = sb("H", [P, D])
        ident = sb("ident", [P, P])
        neg_ident = sb("neg_ident", [P, P])
        ident_b = sb("ident_b", [P, P], bf16)
        row_index = sb("row_index", [P, P])
        node_base = sb("node_base", [P, NODE_TILES + 1])
        bias_rows = sb("bias_rows", [3, HALF], bf16)
        ones_b = sb("ones_b", [P, P], bf16)
        ones_col = sb("ones_col", [P, 1])
        beta_col = sb("beta_col", [P, 1])
        eps_col = sb("eps_col", [P, 1])
        slab_col = sb("slab_col", [P, 1])

        src_idx = [sb(f"src_idx{k}", [P, SUB], i32) for k in range(SLOTS)]
        x_src = [sb(f"x_src{k}", [P, SUB, D]) for k in range(SLOTS)]
        attr = [sb(f"attr{k}", [P, SUB, D]) for k in range(SLOTS)]
        score = sb("score", [P, CHUNK])
        run_max = [sb(f"run_max{k}", [P, 1 + CHUNK]) for k in range(SLOTS)]
        shifted = [sb(f"shifted{k}", [P, CHUNK]) for k in range(SLOTS)]
        weight = sb("weight", [P, CHUNK])
        decay = sb("decay", [P, CHUNK])
        weighted = sb("weighted", [P, CHUNK])
        den = [sb(f"den{k}", [P, CHUNK]) for k in range(SLOTS)]
        num = [sb(f"num{k}", [P, CHUNK]) for k in range(SLOTS)]
        inv_den = sb("inv_den", [P, CHUNK])
        agg = sb("agg", [P, CHUNK])

        x_in = sb("x_in", [P, 2, SUB, D])
        resid = sb("resid", [P, 2, SUB, D])
        out_sb = sb("out_sb", [P, 2, SUB, D])
        pick = sb("pick", [P, 2, SUB, 2, P])
        pick_more = sb("pick_more", [P, P])
        node_ids = sb("node_ids", [P, TILES_IN_SLAB, P])
        stats = sb("stats", [P, TILES_IN_SLAB, 6])
        mean_gap = sb("mean_gap", [P, TILES_IN_SLAB])
        mean_sum = sb("mean_sum", [P, TILES_IN_SLAB])
        sq_sum = sb("sq_sum", [P, TILES_IN_SLAB])
        gap_sq = sb("gap_sq", [P, TILES_IN_SLAB])
        var4 = sb("var4", [P, TILES_IN_SLAB])
        log_var = sb("log_var", [P, TILES_IN_SLAB])
        rstd = sb("rstd", [P, TILES_IN_SLAB])
        shift = sb("shift", [P, TILES_IN_SLAB])

        tile_dst = sb("tile_dst", [HEAP, 2, P + 1])
        tile_dst_i = num[0][0:HEAP, 0:2 * (P + 1)].bitcast(i32).rearrange("q (h e) -> q h e", h=2)
        chunk_dst_i = out_sb[0:CHUNKS, :, :, :].rearrange("p a b c -> p (a b c)")[:, 0:CHUNK + 1].bitcast(i32)
        chunk_dst = resid[0:CHUNKS, :, :, :].rearrange("p a b c -> p (a b c)")[:, 0:CHUNK + 1]
        starts = weighted[0:CHUNKS, :]
        keep = den[0][0:HEAP, 0:2 * P].rearrange("q (h e) -> q h e", h=2)
        passed = pick[0:HEAP, :, :, :, :].rearrange("p a b c d -> p (a b c d)")[:, 0:4 * NODE_TILES] \
            .rearrange("p (a h n) -> p a h n", a=2, h=2)
        iota_i = inv_den[:, 0:P].bitcast(i32)
        base_i = agg[:, 0:NODE_TILES + 1].bitcast(i32)
        part_i = weight[:, 0:1].bitcast(i32)
        part_index = sb("part_index", [P, 1])
        ids_i = x_in[:, :, :, :].rearrange("p a b c -> p (a b) c").bitcast(i32)
        rule = den[1][:, 0:PH * PH].rearrange("p (n j) -> p n j", n=PH)
        W_rep = den[2][:, 0:PH * KR].rearrange("p (n b) -> p n b", n=PH)
        kron = num[1][:, 0:PH * D].rearrange("p (n j b) -> p n j b", n=PH, j=PH)
        bias_in = score[0:1, :]
        bias_parts = sb("bias_parts", [1, 3, HALF], bf16)
        counts = num[2][0:1, 0:NODE_TILES]
        counts_end = decay[0:1, 0:NODE_TILES]
        spans = weighted[0:1, 0:NODE_TILES]
        spans_cum = shifted[0][0:1, 0:NODE_TILES]
        zeros_row = shifted[1][0:1, 0:NODE_TILES]

        msg_t = [pb(f"msg_t{k}", [P, CHUNK]) for k in range(SLOTS)]
        cap = pb("cap", [P, CHUNK])
        decay_arg = pb("decay_arg", [P, CHUNK])
        z_psum = pb("z_psum", [P, SUB, D])
        node_sum = [pb(f"node_sum{h}", [P, SUB, D]) for h in range(2)]

        consts_loaded = sem("consts_loaded")
        rows_moved = sem("rows_moved")
        iotas_made = sem("iotas_made")
        setup_step = sem("setup_step")
        setup_pe = sem("setup_pe")
        idx_loaded = [sem(f"idx_loaded{k}") for k in range(SLOTS)]
        attr_loaded = [sem(f"attr_loaded{k}") for k in range(SLOTS)]
        x_gathered = [sem(f"x_gathered{k}") for k in range(SLOTS)]
        msg_ready = sem("msg_ready")
        cap_ready = sem("cap_ready")
        score_ready = sem("score_ready")
        carry_ready = sem("carry_ready")
        max_ready = sem("max_ready")
        shifted_ready = sem("shifted_ready")
        decay_arg_ready = sem("decay_arg_ready")
        weight_ready = sem("weight_ready")
        decay_ready = sem("decay_ready")
        weighted_ready = sem("weighted_ready")
        den_ready = sem("den_ready")
        num_ready = sem("num_ready")
        log_den_ready = sem("log_den_ready")
        inv_den_ready = sem("inv_den_ready")
        agg_ready = sem("agg_ready")
        z_ready = sem("z_ready")
        z_stored = sem("z_stored")
        pick_ready = sem("pick_ready")
        ids_ready = sem("ids_ready")
        more_ready = sem("more_ready")
        more_used = sem("more_used")
        node_sum_ready = sem("node_sum_ready")
        resid_ready = sem("resid_ready")
        stats_step = sem("stats_step")
        log_var_ready = sem("log_var_ready")
        rstd_ready = sem("rstd_ready")
        normalized = sem("normalized")
        x_loaded = [sem(f"x_loaded{h}") for h in range(2)]
        out_free = sem("out_free")
        out_stored = [sem(f"out_stored{h}") for h in range(2)]
        x_tail_loaded = sem("x_tail_loaded")
        tail_stored = sem("tail_stored")

        STATS_STEPS = 7
        SETUP_SCHEDULE, SETUP_MASKED, SETUP_OPERANDS, SETUP_ALL = 21, 31, 47, 59

        class Count:
            count = 0

            def one(self):
                self.count += 1
                return 1

        def stand_alone(engine):
            engine.nop(nofuse=True)

        def slabs(g):
            return g + 1

        def halves(g, h):
            return 2 * (g + 1) + h

        def through(c):
            return c + SLOTS + 1

        def chunk_of(q, r, lag):
            slot = (r - lag) % SLOTS
            turn = q + (r - lag) // SLOTS
            return turn * SLOTS + slot, turn, slot

        def exists(c):
            return not isinstance(c, int) or 0 <= c < CHUNKS

        def iterate(engine, iteration):
            for i in range(PROLOGUE * SLOTS):
                iteration(i // SLOTS, i % SLOTS)
            with engine.Fori(PROLOGUE, CHUNKS // SLOTS) as q:
                for r in range(SLOTS):
                    iteration(q, r)
            for i in range(CHUNKS // SLOTS * SLOTS, ITERATIONS):
                iteration(i // SLOTS, i % SLOTS)

        def run_slabs(engine, bounds, slab):
            if bounds is None:
                return
            low, high = bounds
            with engine.If(low < high):
                with engine.Fori(low, high) as g:
                    slab(g)

        def slab_bounds(engine, q, r):
            i = q * SLOTS + r
            if isinstance(i, int) and i < FIRST_SLABS:
                return None
            low = engine.value_load(slab_schedule[0:1, bass.ds(i, 1)], min_val=0, max_val=SLABS - 1)
            high = engine.value_load(slab_schedule[0:1, bass.ds(i + 1, 1)], min_val=0, max_val=SLABS - 1)
            return low, high

        def remaining_slabs(engine, slab):
            low = engine.value_load(slab_schedule[0:1, ITERATIONS:ITERATIONS + 1], min_val=0, max_val=SLABS - 1)
            run_slabs(engine, (low, SLABS - 1), slab)

        def further_tiles(engine, wide, g, h, step):
            with engine.If(wide > 2):
                for j in range(SUB):
                    n = g * TILES_IN_SLAB + h * SUB + j
                    first = engine.value_load(first_tile[0:1, bass.ds(n, 1)], min_val=0, max_val=EDGE_TILES - 1)
                    end = engine.value_load(end_tile[0:1, bass.ds(n, 1)], min_val=0, max_val=EDGE_TILES)
                    before = engine.value_load(extra_before[0:1, bass.ds(n, 1)], min_val=0, max_val=1023)
                    with engine.If(first + 2 < end):
                        with engine.Fori(0, end - first - 2) as k:
                            e = (first + 2 + k).with_bounds(min_val=2, max_val=EDGE_TILES - 1)
                            step(j, n, e, before + k)

        block = ctx.enter_context(nc.Block())

        SETUP_DMAS = 3 + 3 + 1 + 2 * PH + 2

        @block.sync
        def _(sp):
            sp.wait_ge(setup_step, 3)
            sp.dma_start(tile_dst_i[:, 0, :], bass.AP(tensor=dst.tensor, offset=0, ap=[[P, HEAP], [1, P + 1]])
                         ).then_inc(consts_loaded, 16)
            sp.dma_start(tile_dst_i[0:HEAP - 1, 1, :],
                         bass.AP(tensor=dst.tensor, offset=HEAP * P, ap=[[P, HEAP - 1], [1, P + 1]])
                         ).then_inc(consts_loaded, 16)
            sp.dma_start(tile_dst_i[HEAP - 1:HEAP, 1, 0:E - (EDGE_TILES - 1) * P],
                         dst[(EDGE_TILES - 1) * P:E].unsqueeze(0)).then_inc(consts_loaded, 16)
            sp.dma_start(chunk_dst_i[0:1, 1:CHUNK + 1], dst[0:CHUNK].unsqueeze(0)).then_inc(consts_loaded, 16)
            sp.dma_start(chunk_dst_i[1:CHUNKS - 1, :],
                         bass.AP(tensor=dst.tensor, offset=CHUNK - 1, ap=[[CHUNK, CHUNKS - 2], [1, CHUNK + 1]])
                         ).then_inc(consts_loaded, 16)
            sp.dma_start(chunk_dst_i[CHUNKS - 1:CHUNKS, 0:TAIL_EDGES + 1],
                         dst[(CHUNKS - 1) * CHUNK - 1:E].unsqueeze(0)).then_inc(consts_loaded, 16)
            sp.dma_start(slab_schedule[0:1, FIRST_SLABS + 1:FIRST_SLABS + CHUNKS], dst[CHUNK:E:CHUNK].unsqueeze(0), allow_slow_non_contiguous=True
                         ).then_inc(consts_loaded, 16)
            for i in range(PH):
                rows = slice(i * KR, (i + 1) * KR)
                sp.dma_start(rule[rows], phm_rule[:, i, :].unsqueeze(0).broadcast_to([KR, PH, PH])
                             ).then_inc(consts_loaded, 16)
                sp.dma_start(W_rep[rows], W.rearrange("n a b -> a n b")).then_inc(consts_loaded, 16)
            sp.dma_start(bias_in.rearrange("o (k d) -> o k d", k=SUB),
                         bias.unsqueeze(0).unsqueeze(0).broadcast_to([1, SUB, D])).then_inc(consts_loaded, 16)
            sp.dma_start(beta_col[:, :], beta.unsqueeze(0).broadcast_to([P, 1])).then_inc(consts_loaded, 16)

            def load_chunk(c, turn, slot, rows=P):
                sp.wait_ge(msg_ready, through(c - SLOTS))
                sp.dma_start(src_idx[slot][0:rows, :],
                             src[bass.ds(c * CHUNK, rows * SUB)].rearrange("(p j) -> p j", j=SUB)
                             ).then_inc(idx_loaded[slot], 16)
                sp.dma_start(attr[slot][0:rows, :, :],
                             edge_attr[bass.ds(c * CHUNK, rows * SUB), :].rearrange("(p j) d -> p j d", j=SUB)
                             ).then_inc(attr_loaded[slot], 16)

            def load_x_half(g, h):
                sp.wait_ge(resid_ready, halves(g, h) - 1)
                sp.dma_start(x_in[:, h, :, :],
                             x[bass.ds(g * SLAB + h * HALF, HALF), :].rearrange("(j p) d -> p j d", p=P)
                             ).then_inc(x_loaded[h], 16)

            def store_half(g, h):
                sp.wait_ge(normalized, halves(g, h) + 1)
                sp.dma_start(out[bass.ds(g * SLAB + h * HALF, HALF), :].rearrange("(j p) d -> p j d", p=P),
                             out_sb[:, h, :, :]).then_inc(out_stored[h], 16)

            def slab(g):
                load_x_half(g + 1, 0)
                load_x_half(g + 1, 1)
                store_half(g, 0)
                store_half(g, 1)
                for h in range(2):
                    sp.wait_ge(out_stored[h], 16 * (g + 1))
                sp.sem_inc(out_free, 1)

            sp.sem_inc(out_free, 1)
            for c in range(2):
                load_chunk(c, 0, c)
            sp.wait_ge(setup_step, SETUP_SCHEDULE)
            load_x_half(0, 0)
            load_x_half(0, 1)

            def iteration(q, r):
                bounds = slab_bounds(sp, q, r)
                c, turn, slot = chunk_of(q, r, -2)
                if isinstance(c, int) and c == CHUNKS - 1:
                    load_chunk(c, turn, slot, TAIL_ROWS)
                elif exists(c):
                    load_chunk(c, turn, slot)
                run_slabs(sp, bounds, slab)

            for i in range(PROLOGUE * SLOTS):
                iteration(i // SLOTS, i % SLOTS)
            with sp.Fori(PROLOGUE, CHUNKS // SLOTS - 1) as q:
                for r in range(SLOTS):
                    iteration(q, r)
            for i in range((CHUNKS // SLOTS - 1) * SLOTS, ITERATIONS):
                iteration(i // SLOTS, i % SLOTS)
            remaining_slabs(sp, slab)

            g = SLABS - 1
            ragged = TAIL_NODES - HALF
            whole, part = ragged // P, ragged % P
            tail = SLABS * SLAB + HALF
            load_x_half(SLABS, 0)
            sp.wait_ge(resid_ready, halves(SLABS, 0))
            sp.dma_start(x_in[:, 1, 0:whole, :], x[tail:tail + whole * P, :].rearrange("(j p) d -> p j d", p=P)
                         ).then_inc(x_loaded[1], 16)
            sp.dma_start(x_in[0:part, 1, whole, :], x[tail + whole * P:N, :]).then_inc(x_tail_loaded, 16)
            store_half(g, 0)
            store_half(g, 1)
            for h in range(2):
                sp.wait_ge(out_stored[h], 16 * SLABS)
            sp.sem_inc(out_free, 1)
            store_half(SLABS, 0)
            sp.wait_ge(normalized, halves(SLABS, 1) + 1)
            sp.dma_start(out[tail:tail + whole * P, :].rearrange("(j p) d -> p j d", p=P),
                         out_sb[:, 1, 0:whole, :]).then_inc(tail_stored, 16)
            sp.dma_start(out[tail + whole * P:N, :], out_sb[0:part, 1, whole, :]).then_inc(tail_stored, 16)
            sp.wait_ge(out_stored[0], 16 * (SLABS + 1))
            sp.wait_ge(out_stored[1], 16 * SLABS)
            sp.wait_ge(tail_stored, 32)

        @block.gpsimd
        def _(pool):
            nc.gpsimd.iota(iota_i, pattern=[[1, P]], base=0, channel_multiplier=0).then_inc(iotas_made, 1)
            nc.gpsimd.iota(part_i, pattern=[[0, 1]], base=0, channel_multiplier=1).then_inc(iotas_made, 1)
            nc.gpsimd.iota(base_i, pattern=[[P, NODE_TILES + 1]], base=0, channel_multiplier=0
                           ).then_inc(iotas_made, 1)
            nc.gpsimd.iota(ids_i, pattern=[[P, TILES_IN_SLAB], [1, P]], base=0, channel_multiplier=0
                           ).then_inc(iotas_made, 1)

            def gather(c, turn, slot):
                pool.wait_ge(idx_loaded[slot], 16 * (turn + 1))
                pool.wait_ge(msg_ready, through(c - SLOTS))
                stand_alone(pool)
                for j in range(SUB):
                    nc.gpsimd.indirect_dma_start(
                        out=x_src[slot][:, j, :], out_offset=None, in_=x[:, :],
                        in_offset=bass.IndirectOffsetOnAxis(ap=src_idx[slot][:, j:j + 1], axis=0),
                    ).then_inc(x_gathered[slot], 16)

            for c in range(SLOTS):
                gather(c, 0, c)
            with pool.Fori(1, CHUNKS // SLOTS) as q:
                for r in range(SLOTS):
                    gather(q * SLOTS + r, q, r)
            for c in range(CHUNKS // SLOTS * SLOTS, CHUNKS):
                gather(c, c // SLOTS, c % SLOTS)

        @block.vector
        def _(dve):
            V = nc.vector
            dve.sem_inc(pick_ready, 2)
            dve.sem_inc(resid_ready, 2)
            dve.sem_inc(stats_step, STATS_STEPS)
            dve.sem_inc(carry_ready, SLOTS)
            dve.sem_inc(max_ready, SLOTS)
            dve.sem_inc(shifted_ready, SLOTS)
            dve.sem_inc(weighted_ready, SLOTS)
            dve.sem_inc(den_ready, SLOTS)
            dve.sem_inc(num_ready, SLOTS)
            dve.sem_inc(agg_ready, SLOTS)

            made = Count()

            V.memset(tile_dst_i, PAD_DST).then_inc(setup_step, made.one())
            V.memset(chunk_dst_i, PAD_DST).then_inc(setup_step, made.one())
            V.memset(slab_schedule[:, :], 0).then_inc(setup_step, made.one())
            V.memset(z[:, EDGE_TILES:, :], 0.0).then_inc(setup_step, made.one())
            V.memset(last_dst[:, EDGE_TILES:], -1.0).then_inc(setup_step, made.one())
            V.memset(edge_rows[:, :, :], 0.0).then_inc(setup_step, made.one())
            V.memset(ones_b[:, :], 1.0).then_inc(setup_step, made.one())
            V.memset(ones_col[:, :], 1.0).then_inc(setup_step, made.one())
            V.memset(eps_col[:, :], EPS).then_inc(setup_step, made.one())
            V.memset(slab_col[:, :], float(SLAB)).then_inc(setup_step, made.one())
            V.memset(run_max[SLOTS - 1][:, CHUNK:], 0.0).then_inc(setup_step, made.one())
            V.memset(zeros_row, 0.0).then_inc(setup_step, made.one())
            dve.wait_ge(iotas_made, 4)
            V.tensor_copy(row_index[:, :], iota_i).then_inc(setup_step, made.one())
            V.tensor_copy(part_index[:, :], part_i).then_inc(setup_step, made.one())
            V.tensor_copy(node_base[:, :], base_i).then_inc(setup_step, made.one())
            V.tensor_copy(node_ids[:, :, :], ids_i).then_inc(setup_step, made.one())
            dve.wait_ge(setup_step, made.count)
            V.tensor_scalar(ident[:, :], row_index[:, :], part_index[:, 0:1], None, op0=ALU.is_equal).then_inc(setup_step, made.one())
            dve.wait_ge(setup_step, made.count)
            V.tensor_scalar(neg_ident[:, :], ident[:, :], -1.0, None, op0=ALU.mult).then_inc(setup_step, made.one())
            V.tensor_copy(ident_b[:, :], ident[:, :]).then_inc(setup_step, made.one())

            dve.wait_ge(consts_loaded, 16 * SETUP_DMAS)
            V.tensor_scalar(slab_schedule[0:1, FIRST_SLABS + 1:FIRST_SLABS + CHUNKS], slab_schedule[0:1, FIRST_SLABS + 1:FIRST_SLABS + CHUNKS],
                                 SLAB.bit_length() - 1, None, op0=ALU.arith_shift_right).then_inc(setup_step, made.one())
            dve.wait_ge(setup_step, made.count)
            V.tensor_scalar(slab_schedule[0:1, FIRST_SLABS + 1:FIRST_SLABS + CHUNKS],
                                            slab_schedule[0:1, FIRST_SLABS + 1:FIRST_SLABS + CHUNKS], float(SLABS - 1), None, op0=ALU.min).then_inc(setup_step, made.one())
            assert made.count == SETUP_SCHEDULE, made.count
            V.tensor_copy(tile_dst[:, :, :], tile_dst_i).then_inc(setup_step, made.one())
            V.tensor_copy(chunk_dst, chunk_dst_i).then_inc(setup_step, made.one())
            dve.wait_ge(setup_step, made.count)
            V.tensor_tensor(starts, chunk_dst[:, 1:CHUNK + 1], chunk_dst[:, 0:CHUNK], op=ALU.is_equal).then_inc(setup_step, made.one())
            V.tensor_tensor(keep, tile_dst[:, :, 0:P], tile_dst[:, :, 1:P + 1], op=ALU.is_equal).then_inc(setup_step, made.one())
            dve.wait_ge(setup_step, made.count)
            V.tensor_scalar(edge_rows[0:CHUNKS, 1, :], starts, -1.0, HUGE, op0=ALU.add, op1=ALU.mult).then_inc(setup_step, made.one())
            V.tensor_scalar(starts, starts, 2.0, -1.0, op0=ALU.mult, op1=ALU.add).then_inc(setup_step, made.one())
            V.tensor_scalar(keep, keep, -1.0, 1.0, op0=ALU.mult, op1=ALU.add).then_inc(setup_step, made.one())
            dve.wait_ge(setup_step, made.count)
            V.tensor_scalar(edge_rows[0:CHUNKS, 0, :], starts, HUGE, None, op0=ALU.mult).then_inc(setup_step, made.one())
            V.scalar_tensor_tensor(keep, tile_dst[:, :, 0:P], 1.0, keep, op0=ALU.add, op1=ALU.mult).then_inc(setup_step, made.one())
            dve.wait_ge(setup_step, made.count)
            V.tensor_scalar(keep, keep, -1.0, None, op0=ALU.add).then_inc(setup_step, made.one())
            assert made.count == SETUP_MASKED, made.count
            for h in range(2):
                V.tensor_scalar(passed[:, 0, h, :], node_base[0:HEAP, 0:NODE_TILES],
                                     tile_dst[:, h, P - 1:P], None, op0=ALU.is_gt).then_inc(setup_step, made.one())
                V.tensor_scalar(passed[:, 1, h, :], node_base[0:HEAP, 1:NODE_TILES + 1],
                                     tile_dst[:, h, 0:1], None, op0=ALU.is_gt).then_inc(setup_step, made.one())
            for n in range(PH):
                V.tensor_tensor(kron[:, n], rule[:, n, :].unsqueeze(2).broadcast_to([P, PH, KR]),
                                     W_rep[:, n, :].unsqueeze(1).broadcast_to([P, PH, KR]), op=ALU.mult).then_inc(setup_step, made.one())
            H_v = H[:, :].rearrange("p (j b) -> p j b", j=PH)
            dve.wait_ge(setup_step, made.count)
            V.tensor_tensor(H_v, kron[:, 0], kron[:, 1], op=ALU.add).then_inc(setup_step, made.one())
            for n in range(2, PH):
                dve.wait_ge(setup_step, made.count)
                V.tensor_tensor(H_v, H_v, kron[:, n], op=ALU.add).then_inc(setup_step, made.one())
            for k in range(3):
                dve.wait_ge(setup_step, made.count)
                V.tensor_copy(bias_parts[:, k, :], bias_in).then_inc(setup_step, made.one())
                if k < 2:
                    dve.wait_ge(setup_step, made.count)
                    V.tensor_tensor(bias_in, bias_in, bias_parts[:, k, :], op=ALU.subtract).then_inc(setup_step, made.one())
            assert made.count == SETUP_OPERANDS, made.count.done
            dve.wait_ge(setup_pe, 4)
            V.tensor_copy(last_dst[:, 0:HEAP], node_sum[0][:, 0, 0:HEAP]).then_inc(setup_step, made.one())
            V.tensor_copy(last_dst[:, HEAP:EDGE_TILES], node_sum[1][:, 0, 0:HEAP]).then_inc(setup_step, made.one())
            V.tensor_copy(counts, cap[0:1, 0:NODE_TILES]).then_inc(setup_step, made.one())
            V.tensor_copy(counts_end, decay_arg[0:1, 0:NODE_TILES]).then_inc(setup_step, made.one())
            dve.wait_ge(setup_step, made.count)
            V.tensor_copy(first_tile[:, :], counts).then_inc(setup_step, made.one())
            V.tensor_copy(end_tile[:, :], counts_end).then_inc(setup_step, made.one())
            V.tensor_tensor(spans, counts_end, counts, op=ALU.subtract).then_inc(setup_step, made.one())
            dve.wait_ge(setup_step, made.count)
            V.tensor_reduce(part_index[0:1, 0:1], spans, op=ALU.max, axis=AX.X).then_inc(setup_step, made.one())
            V.tensor_scalar(spans, spans, -2.0, 0.0, op0=ALU.add, op1=ALU.max).then_inc(setup_step, made.one())
            dve.wait_ge(setup_step, made.count)
            V.tensor_copy(wide_flag[:, :], part_index[0:1, 0:1]).then_inc(setup_step, made.one())
            V.tensor_tensor_scan(spans_cum, spans, zeros_row, initial=0.0, op0=ALU.add, op1=ALU.add).then_inc(setup_step, made.one())
            dve.wait_ge(setup_step, made.count)
            V.tensor_tensor(extra_before[:, :], spans_cum, spans, op=ALU.subtract).then_inc(setup_step, made.one())
            assert made.count == SETUP_ALL, made.count.done
            dve.wait_ge(setup_step, made.count)
            wide = dve.value_load(wide_flag[0:1, 0:1], min_val=0, max_val=EDGE_TILES)
            regs = [dve.alloc_register(f"dve_first{j}") for j in range(TILES_IN_SLAB)]

            def load_firsts(g):
                dve.load(regs, first_tile[0:1, bass.ds(g * TILES_IN_SLAB, TILES_IN_SLAB)])

            def build_picks(g, h):
                dve.wait_ge(ids_ready, slabs(g))
                dve.wait_ge(node_sum_ready, halves(g, h) - 1)
                for j in range(SUB):
                    first = dve.snap(regs[h * SUB + j], min_val=0, max_val=EDGE_TILES - 1)
                    made = V.tensor_tensor(
                        pick[:, h, j, :, :],
                        node_ids[:, h * SUB + j, :].unsqueeze(1).broadcast_to([P, 2, P]),
                        last_dst[:, bass.ds(first, 2)].unsqueeze(2).broadcast_to([P, 2, P]),
                        op=ALU.is_equal)
                made.then_inc(pick_ready, 1)

            load_firsts(0)
            build_picks(0, 0)
            build_picks(0, 1)

            def slab(g):
                more_slabs = not isinstance(g, int) or g < SLABS
                if more_slabs:
                    load_firsts(g + 1)
                for h in range(2):
                    def more(j, n, e, before):
                        dve.wait_ge(more_used, 1 + before)
                        V.tensor_scalar(pick_more[:, :], row_index[:, :], node_base[:, bass.ds(n, 1)],
                                        last_dst[:, bass.ds(e, 1)], op0=ALU.add, op1=ALU.is_equal
                                        ).then_inc(more_ready, 1)
                    further_tiles(dve, wide, g, h, more)
                    dve.wait_ge(node_sum_ready, halves(g, h) + 1)
                    dve.wait_ge(x_loaded[h], 16 * (g + 1))
                    if isinstance(g, int) and g == SLABS and h == 1:
                        dve.wait_ge(x_tail_loaded, 16)
                    dve.wait_ge(normalized, halves(g, 0))
                    V.scalar_tensor_tensor(resid[:, h, :, :], x_in[:, h, :, :], 2.0, node_sum[h][:, :, :],
                                           op0=ALU.mult, op1=ALU.add).then_inc(resid_ready, 1)
                    dve.wait_ge(resid_ready, halves(g, h) + 1)
                    dve.wait_ge(stats_step, STATS_STEPS * slabs(g))
                    for j in range(SUB):
                        bn = V.bn_stats(stats[:, h * SUB + j, :], resid[:, h, j, :])
                bn.then_inc(stats_step, 1)
                done = STATS_STEPS * slabs(g)
                dve.wait_ge(stats_step, done + 1)
                dve.wait_ge(log_var_ready, slabs(g))
                V.tensor_tensor(mean_gap[:, :], stats[:, :, 1], stats[:, :, 4], op=ALU.subtract).then_inc(stats_step, 1)
                V.tensor_tensor(mean_sum[:, :], stats[:, :, 1], stats[:, :, 4], op=ALU.add).then_inc(stats_step, 1)
                V.tensor_tensor(sq_sum[:, :], stats[:, :, 2], stats[:, :, 5], op=ALU.add).then_inc(stats_step, 1)
                dve.wait_ge(stats_step, done + 2)
                V.tensor_tensor(gap_sq[:, :], mean_gap[:, :], mean_gap[:, :], op=ALU.mult).then_inc(stats_step, 1)
                dve.wait_ge(stats_step, done + 5)
                V.scalar_tensor_tensor(var4[:, :], sq_sum[:, :], 4.0 / D, gap_sq[:, :],
                                       op0=ALU.mult, op1=ALU.add).then_inc(stats_step, 1)
                if more_slabs:
                    build_picks(g + 1, 0)
                dve.wait_ge(rstd_ready, slabs(g) + 1)
                dve.wait_ge(normalized, halves(g, 0))
                V.scalar_tensor_tensor(shift[:, :], mean_sum[:, :], -0.5, rstd[:, :],
                                       op0=ALU.mult, op1=ALU.mult).then_inc(stats_step, 1)
                if more_slabs:
                    build_picks(g + 1, 1)

            def iteration(q, r):
                bounds = slab_bounds(dve, q, r)
                c, turn, s = chunk_of(q, r, 2)
                if exists(c):
                    dve.wait_ge(weight_ready, through(c))
                    dve.wait_ge(num_ready, through(c - 1))
                    V.tensor_tensor(weighted[:, :], msg_t[s][:, :], weight[:, :], op=ALU.mult
                                    ).then_inc(weighted_ready, 1)
                c, turn, s = chunk_of(q, r, 1)
                if exists(c):
                    before = run_max[(s - 1) % SLOTS]
                    dve.wait_ge(max_ready, through(c - 1))
                    dve.wait_ge(decay_arg_ready, through(c - SLOTS))
                    V.tensor_copy(run_max[s][:, 0:1], before[:, CHUNK:]).then_inc(carry_ready, 1)
                    dve.wait_ge(score_ready, through(c))
                    dve.wait_ge(cap_ready, through(c))
                    V.tensor_tensor_scan(run_max[s][:, 1:], cap[:, :], score[:, :], initial=before[:, CHUNK:],
                                         op0=ALU.min, op1=ALU.max).then_inc(max_ready, 1)
                    dve.wait_ge(max_ready, through(c))
                    dve.wait_ge(weight_ready, through(c - SLOTS))
                    V.tensor_tensor(shifted[s][:, :], score[:, :], run_max[s][:, 1:], op=ALU.subtract
                                    ).then_inc(shifted_ready, 1)
                c, turn, s = chunk_of(q, r, 2)
                has_sums = exists(c)
                if has_sums:
                    dve.wait_ge(decay_ready, through(c))
                    dve.wait_ge(den_ready, through(c - 1))
                    dve.wait_ge(log_den_ready, through(c - SLOTS))
                    first = isinstance(c, int) and c == 0
                    V.tensor_tensor_scan(den[s][:, :], decay[:, :], weight[:, :],
                                         initial=0.0 if first else den[(s - 1) % SLOTS][:, CHUNK - 1:],
                                         op0=ALU.mult, op1=ALU.add).then_inc(den_ready, 1)
                    dve.wait_ge(weighted_ready, through(c))
                    dve.wait_ge(agg_ready, through(c - SLOTS))
                    V.tensor_tensor_scan(num[s][:, :], decay[:, :], weighted[:, :],
                                         initial=0.0 if first else num[(s - 1) % SLOTS][:, CHUNK - 1:],
                                         op0=ALU.mult, op1=ALU.add).then_inc(num_ready, 1)
                run_slabs(dve, bounds, slab)
                if has_sums:
                    dve.wait_ge(inv_den_ready, through(c))
                    dve.wait_ge(num_ready, through(c))
                    dve.wait_ge(z_ready, through(c - 1))
                    V.tensor_tensor(agg[:, :], num[s][:, :], inv_den[:, :], op=ALU.mult).then_inc(agg_ready, 1)

            iterate(dve, iteration)
            remaining_slabs(dve, slab)
            slab(SLABS - 1)
            slab(SLABS)

        @block.scalar
        def _(act):
            A = nc.scalar
            act.sem_inc(ids_ready, 1)
            act.sem_inc(log_var_ready, 1)
            act.sem_inc(rstd_ready, 1)
            act.sem_inc(normalized, 2)
            act.sem_inc(score_ready, SLOTS)
            act.sem_inc(weight_ready, SLOTS)
            act.sem_inc(decay_ready, SLOTS)
            act.sem_inc(log_den_ready, SLOTS)
            act.sem_inc(inv_den_ready, SLOTS)
            act.sem_inc(z_stored, SLOTS)
            act.wait_ge(setup_step, SETUP_OPERANDS)
            A.preload_act_table_set("natural_log_exp_and_others")
            for k in range(3):
                act.dma_start(bias_rows[k:k + 1, :], bias_parts[:, k, :]).then_inc(rows_moved, 16)
            act.wait_ge(setup_step, SETUP_ALL)

            def slab(g):
                if not isinstance(g, int) or g < SLABS:
                    act.wait_ge(pick_ready, halves(g, 1) + 1)
                    act.wait_ge(ids_ready, slabs(g))
                    A.activation(node_ids[:, :, :], node_ids[:, :, :], ACT.Identity, bias=slab_col[:, 0:1]
                                 ).then_inc(ids_ready, 1)
                act.wait_ge(stats_step, STATS_STEPS * slabs(g) + 6)
                act.wait_ge(rstd_ready, slabs(g))
                A.activation(log_var[:, :], var4[:, :], ACT.Ln, bias=eps_col[:, 0:1], scale=0.25
                             ).then_inc(log_var_ready, 1)
                act.wait_ge(log_var_ready, slabs(g) + 1)
                act.wait_ge(normalized, halves(g, 0))
                A.activation(rstd[:, :], log_var[:, :], ACT.Exp, scale=-0.5).then_inc(rstd_ready, 1)
                act.wait_ge(stats_step, STATS_STEPS * slabs(g) + 7)
                act.wait_ge(out_free, slabs(g))
                for h in range(2):
                    for j in range(SUB):
                        t = h * SUB + j
                        norm = A.activation(out_sb[:, h, j, :], resid[:, h, j, :], ACT.Identity,
                                            bias=shift[:, t:t + 1], scale=rstd[:, t:t + 1])
                    norm.then_inc(normalized, 1)

            def iteration(q, r):
                bounds = slab_bounds(act, q, r)
                c, turn, s = chunk_of(q, r, 3)
                if exists(c):
                    act.wait_ge(z_ready, through(c))
                    A.activation(z[:, bass.ds(c * SUB, SUB), :], z_psum[:, :, :], ACT.Copy).then_inc(z_stored, 1)
                c, turn, s = chunk_of(q, r, 2)
                if exists(c):
                    act.wait_ge(den_ready, through(c))
                    act.wait_ge(agg_ready, through(c - 1))
                    A.activation(inv_den[:, :], den[s][:, :], ACT.Ln).then_inc(log_den_ready, 1)
                    act.wait_ge(log_den_ready, through(c))
                    A.activation(inv_den[:, :], inv_den[:, :], ACT.Exp, scale=-1.0).then_inc(inv_den_ready, 1)
                c, turn, s = chunk_of(q, r, 1)
                has_weights = exists(c)
                if has_weights:
                    act.wait_ge(shifted_ready, through(c))
                    act.wait_ge(den_ready, through(c - 1))
                    act.wait_ge(weighted_ready, through(c - 1))
                    A.activation(weight[:, :], shifted[s][:, :], ACT.Exp).then_inc(weight_ready, 1)
                now, turn, s = chunk_of(q, r, 0)
                if exists(now):
                    act.wait_ge(msg_ready, through(now))
                    act.wait_ge(shifted_ready, through(now - 1))
                    A.activation(score[:, :], msg_t[s][:, :], ACT.Identity, scale=beta_col[:, 0:1]
                                 ).then_inc(score_ready, 1)
                run_slabs(act, bounds, slab)
                if has_weights:
                    act.wait_ge(decay_arg_ready, through(c))
                    act.wait_ge(num_ready, through(c - 1))
                    A.activation(decay[:, :], decay_arg[:, :], ACT.Exp).then_inc(decay_ready, 1)

            iterate(act, iteration)
            remaining_slabs(act, slab)
            slab(SLABS - 1)
            slab(SLABS)

        @block.tensor
        def _(pe):
            T = nc.tensor
            pe.sem_inc(node_sum_ready, 2)
            pe.sem_inc(more_used, 1)
            pe.sem_inc(msg_ready, SLOTS)
            pe.sem_inc(cap_ready, SLOTS)
            pe.sem_inc(decay_arg_ready, SLOTS)
            pe.sem_inc(z_ready, SLOTS)
            pe.wait_ge(setup_step, SETUP_OPERANDS)
            for h in range(2):
                T.transpose(node_sum[h][:, 0, 0:HEAP], keep[:, h, :], ident[0:HEAP, 0:HEAP]).then_inc(setup_pe, 1)
            for a, counted in enumerate((cap, decay_arg)):
                for h in range(2):
                    sums = T.matmul(counted[0:1, 0:NODE_TILES], ones_col[0:HEAP, :], passed[:, a, h, :],
                                    start=(h == 0), stop=(h == 1))
                sums.then_inc(setup_pe, 1)
            pe.wait_ge(setup_step, SETUP_ALL)
            pe.wait_ge(rows_moved, 48)
            wide = pe.value_load(wide_flag[0:1, 0:1], min_val=0, max_val=EDGE_TILES)
            regs = [pe.alloc_register(f"pe_first{j}") for j in range(TILES_IN_SLAB)]

            def broadcast_row(target, c, row, stop):
                return T.matmul(target[:, :], ident_b[:, bass.ds(c, 1)].broadcast_to([P, P]), edge_rows[:, row, :],
                                start=True, stop=stop)

            def load_firsts(g):
                pe.load(regs, first_tile[0:1, bass.ds(g * TILES_IN_SLAB, TILES_IN_SLAB)])

            load_firsts(0)

            def slab(g, stored=through(CHUNKS - 1)):
                firsts = [pe.snap(reg, min_val=0, max_val=EDGE_TILES - 1) for reg in regs]
                for h in range(2):
                    pe.wait_ge(resid_ready, halves(g, 0))
                    T.matmul(node_sum[h][:, :, :], ones_b[0:3, :], bias_rows[:, :], start=True, stop=False)
                    pe.wait_ge(z_stored, stored)

                    def more(j, n, e, before):
                        pe.wait_ge(more_ready, before + 1)
                        T.matmul(node_sum[h][:, j, :], pick_more[:, :], z[:, bass.ds(e, 1), :],
                                 start=False, stop=False).then_inc(more_used, 1)
                    further_tiles(pe, wide, g, h, more)
                    pe.wait_ge(pick_ready, halves(g, h) + 1)
                    for j in range(SUB):
                        for k in range(2):
                            picked = T.matmul(node_sum[h][:, j, :], pick[:, h, j, k, :],
                                              z[:, bass.ds(firsts[h * SUB + j] + k, 1), :],
                                              start=False, stop=(j == SUB - 1 and k == 1))
                    picked.then_inc(node_sum_ready, 1)
                if not isinstance(g, int) or g < SLABS:
                    stand_alone(pe)
                    load_firsts(g + 1)

            def iteration(q, r):
                bounds = slab_bounds(pe, q, r)
                c, turn, s = chunk_of(q, r, 0)
                if exists(c):
                    pe.wait_ge(attr_loaded[s], 16 * (turn + 1))
                    pe.wait_ge(x_gathered[s], 16 * SUB * (turn + 1))
                    pe.wait_ge(weighted_ready, through(c - SLOTS))
                    pe.wait_ge(score_ready, through(c - SLOTS))
                    for j in range(SUB):
                        turned = msg_t[s][:, :].rearrange("d (p j) -> d p j", j=SUB)[:, :, j]
                        T.matmul(turned, x_src[s][:, j, :], ident[:, :], start=True, stop=False)
                        msg = T.matmul(turned, attr[s][:, j, :], ident[:, :], start=False, stop=True)
                    msg.then_inc(msg_ready, 1)
                c, turn, s = chunk_of(q, r, 3)
                if exists(c):
                    pe.wait_ge(agg_ready, through(c))
                    pe.wait_ge(z_stored, through(c - 1))
                    for k in range(SUB):
                        prod = T.matmul(z_psum[:, k, :], agg[:, k * P:(k + 1) * P], H[:, :], start=True, stop=True)
                    prod.then_inc(z_ready, 1)
                c, turn, s = chunk_of(q, r, 4)
                stored = through(c if exists(c) else CHUNKS - 1)
                run_slabs(pe, bounds, lambda g: slab(g, stored))
                c, turn, s = chunk_of(q, r, 1)
                if exists(c):
                    pe.wait_ge(max_ready, through(c))
                    pe.wait_ge(carry_ready, through(c))
                    pe.wait_ge(decay_ready, through(c - 1))
                    broadcast_row(decay_arg, c, 1, False)
                    T.matmul(decay_arg[:, :], ident[:, :], run_max[s][:, 0:CHUNK], start=False, stop=False)
                    T.matmul(decay_arg[:, :], neg_ident[:, :], run_max[s][:, 1:CHUNK + 1], start=False, stop=True
                             ).then_inc(decay_arg_ready, 1)
                c, turn, s = chunk_of(q, r, 0)
                if exists(c):
                    pe.wait_ge(max_ready, through(c - 1))
                    broadcast_row(cap, c, 0, True).then_inc(cap_ready, 1)

            iterate(pe, iteration)
            remaining_slabs(pe, slab)
            slab(SLABS - 1)
            slab(SLABS)


_INS = ["x", "src", "dst", "edge_attr_128", "L0_gnn_phm_rule", "L0_gnn_W", "L0_gnn_bias", "L0_gnn_beta"]
_OUT = ((50000, 128), "float32")


def kernel(**inputs):
    import numpy as _np
    import concourse.bacc as _bacc
    from concourse import mybir as _mybir
    from concourse.bass_utils import run_bass_kernel_spmd as _run

    nc = _bacc.Bacc("TRN2", target_bir_lowering=False, num_devices=1)
    arrays, args = {}, []
    for name in _INS:
        a = _np.ascontiguousarray(inputs[name])
        a = a.reshape(a.shape or (1,))
        arrays[f"in_{name}_dram"] = a
        args.append(nc.dram_tensor(f"in_{name}_dram", a.shape, _mybir.dt.from_np(a.dtype), kind="ExternalInput").ap())
    dt = _mybir.dt.from_np(_np.dtype(_OUT[1]))
    args.append(nc.dram_tensor("out_0_dram", _OUT[0], dt, kind="ExternalOutput").ap())
    gnn_kernel(nc, *args)
    r = _run(nc, [arrays], core_ids=[0])
    return r.results[0]["out_0_dram"]
```
